# Optimizing a Trainium2 kernel written in Bass

```python
import numpy as np
import jax
import jax.numpy as jnp

def _softmax(x, axis=-1):
    return jax.nn.softmax(x, axis=axis)

def _gelu(x):
    return jax.nn.gelu(x, approximate=True)

def _silu(x):
    return jax.nn.silu(x)

def _sigmoid(x):
    return jax.nn.sigmoid(x)

def _layernorm(x, axis=-1, eps=1e-05):
    m = jnp.mean(x, axis=axis, keepdims=True)
    v = jnp.var(x, axis=axis, keepdims=True)
    return (x - m) / jnp.sqrt(v + eps)

def _scatter_add(tgt, idx, src, axis=0):
    return tgt.at[idx].add(src)

def _segment_sum(src, seg, n):
    return jax.ops.segment_sum(src, seg, n)
kernel_name = 'mk_cond_resid_d1_seqx_r2_45fdf4'

def setup_inputs(seed: int=0):
    np.random.seed(seed)
    _w = jnp.asarray

    def _rec_inputs():
        import jax
        import jax.numpy as jnp
        _rk = jax.random.key(seed)
        x = -0.000125 + 0.9999 * jax.random.normal(jax.random.fold_in(_rk, 1), (32, 512, 512), jnp.float32)
        _lenS = 512 - jax.random.randint(jax.random.fold_in(_rk, 7), (32,), 0, max(1, 512 // 4) + 1, jnp.int32)
        _lenS2 = 512 - jax.random.randint(jax.random.fold_in(_rk, 8), (32,), 0, max(1, 512 // 4) + 1, jnp.int32)
        cond_1024 = -0.00493535 + 1.00056 * jax.random.normal(jax.random.fold_in(_rk, 11), (32, 512), jnp.float32)
        return (x, cond_1024)
    x, cond_1024 = _rec_inputs()

    def _L0_cond_setup():
        import jax, jax.numpy as jnp
        import numpy as np
        import math
        N, T, D, H = (64, 256, 512, 512)
        key = jax.random.key(seed)
        k1, k2, k3, k4 = jax.random.split(key, 4)
        x = jax.random.normal(k1, (N, T, D), dtype=jnp.float32)
        h0 = jax.random.normal(k2, (N, H), dtype=jnp.float32)
        Wx = jax.random.normal(k3, (D, 4 * H), dtype=jnp.float32) / math.sqrt(D)
        Wh = jax.random.normal(k4, (H, 4 * H), dtype=jnp.float32) / math.sqrt(H)
        b = jnp.zeros((4 * H,), dtype=jnp.float32)
        return {'x': x, 'h0': h0, 'Wx': Wx, 'Wh': Wh, 'b': b}
    _L0_cond_all = _L0_cond_setup()
    _L0_cond_in = {k: v for k, v in _L0_cond_all.items() if k in ('Wx', 'Wh', 'b')}
    del _L0_cond_all
    return {'x': x, 'cond_1024': cond_1024, 'L0_cond_Wx': _L0_cond_in['Wx'], 'L0_cond_Wh': _L0_cond_in['Wh'], 'L0_cond_b': _L0_cond_in['b']}

def reference(x, cond_1024, L0_cond_Wx, L0_cond_Wh, L0_cond_b):
    import jax
    import jax.numpy as jnp

    def _L0_cond_ref(x, h0, Wx, Wh, b):
        import jax, jax.numpy as jnp
        import numpy as np
        import math
        N, T, D, H = (64, 256, 512, 512)
        Hdim = h0.shape[1]
        c0 = jnp.zeros_like(h0)
        xW = jnp.einsum('ntd,dk->tnk', x, Wx) + b

        def step(carry, xw_t):
            prev_h, prev_c = carry
            a = xw_t + prev_h @ Wh
            i = jax.nn.sigmoid(a[:, :Hdim])
            f = jax.nn.sigmoid(a[:, Hdim:2 * Hdim])
            o = jax.nn.sigmoid(a[:, 2 * Hdim:3 * Hdim])
            g = jnp.tanh(a[:, 3 * Hdim:])
            next_c = f * prev_c + i * g
            next_h = o * jnp.tanh(next_c)
            return ((next_h, next_c), next_h)
        _, hs = jax.lax.scan(step, (h0, c0), xW)
        return jnp.transpose(hs, (1, 0, 2))
    x = x + _L0_cond_ref(x, cond_1024, L0_cond_Wx, L0_cond_Wh, L0_cond_b)
    return x

_drawn_inputs = setup_inputs


def setup_inputs(seed=0):
    import zlib

    import numpy as np

    out = dict(_drawn_inputs(seed))
    spreads = {'L0_cond_b': (0.0, 0.1)}
    factors = {}
    for name, (base, spread) in spreads.items():
        noise = np.random.default_rng([zlib.crc32(name.encode()), seed]).standard_normal(out[name].shape)
        drawn = base * np.exp(spread * noise) if base else spread * noise
        out[name] = jnp.asarray(drawn.astype(out[name].dtype))
    for name, factor in factors.items():
        out[name] = (out[name] * factor).astype(out[name].dtype)
    return out
```

```python
from contextlib import ExitStack

import concourse.bass as bass
from concourse import mybir

ALU = mybir.AluOpType
ACT = mybir.ActivationFunctionType
F32 = mybir.dt.float32
F16 = mybir.dt.float16

P = 128
GATES = 4
WSCALE = 64.0
CHUNK = 16
SLOTS = 4
HEAD = 8


def lstm_residual(nc, x, h0, w_x, w_h, bias, out):
    N, T, D = x.shape
    H = h0.shape[1]
    J = D // P
    assert D == H and J * N == P and w_x.shape[1] == GATES * H
    G = GATES * P
    RING = CHUNK * SLOTS
    assert T % RING == 0 and T >= 2 * RING
    CHUNKS = T // CHUNK
    UNSCALE = 1.0 / WSCALE

    x_v = [x[:, :, j * P:(j + 1) * P] for j in range(J)]
    out_v = [out[:, :, j * P:(j + 1) * P] for j in range(J)]
    w_v = [w[k * P:(k + 1) * P, :] for w in (w_x, w_h) for k in range(J)]

    with ExitStack() as ctx:
        def sb(name, shape, dt):
            return ctx.enter_context(nc.sbuf_tensor(name, shape, dt))

        def psum(name, shape, dt):
            return ctx.enter_context(nc.psum_tensor(name, shape, dt))

        def sem(name):
            return ctx.enter_context(nc.semaphore(name))

        w_hi = sb("w_hi", [P, 2, J, J, G], F16)
        w_lo = sb("w_lo", [P, 2, J, J, G], F16)
        w_raw = sb("w_raw", [P, 2 * J, GATES * H], F32)
        bias_raw = sb("bias_raw", [P, G], F32)
        bias_sc = sb("bias_sc", [P, G], F32)
        ident = sb("ident", [P, P], F16)
        x_ring = sb("x_ring", [P, RING * P], F32)
        h0_raw = sb("h0_raw", [P, P], F32)
        x_parts = sb("x_parts", [P, 2, 2, P], F16)
        xT = sb("xT", [P, 2, 2, P], F16)
        h_hi = sb("h_hi", [P, P], F16)
        h_lo = sb("h_lo", [P, P], F16)
        h_full = sb("h_full", [P, P], F32)
        hT_hi = sb("hT_hi", [P, P], F16)
        hT_lo = sb("hT_lo", [P, P], F16)
        i_f = sb("i_f", [P, 2 * P], F32)
        o_gate = sb("o_gate", [P, P], F32)
        g_c = sb("g_c", [P, 2 * P], F32)
        prods = sb("prods", [P, 2 * P], F32)
        tanh_c = sb("tanh_c", [P, P], F32)

        gates = [psum(f"gates{p}", [P, G], F32) for p in range(2)]
        xT_ps = [psum(f"xT_ps{p}", [P, 2 * P], F16) for p in range(2)]
        hT_hi_ps = psum("hT_hi_ps", [P, P], F16)
        hT_lo_ps = psum("hT_lo_ps", [P, P], F16)

        w_loaded = [sem(f"w_loaded{n}") for n in range(2 * J)]
        small_loaded = sem("small_loaded")
        ident_zeroed = sem("ident_zeroed")
        ident_ready = sem("ident_ready")
        w_hi_ready = sem("w_hi_ready")
        w_lo_ready = sem("w_lo_ready")
        bias_ready = sem("bias_ready")
        banks_open = sem("banks_open")
        c_zeroed = sem("c_zeroed")
        x_loaded = sem("x_loaded")
        out_stored = sem("out_stored")
        x_hi_ready = sem("x_hi_ready")
        x_lo_ready = sem("x_lo_ready")
        xT_in_psum = sem("xT_in_psum")
        xT_ready = sem("xT_ready")
        seeded = sem("seeded")
        gates_ready = sem("gates_ready")
        ifg_ready = sem("ifg_ready")
        o_ready = sem("o_ready")
        prods_ready = sem("prods_ready")
        c_ready = sem("c_ready")
        tanh_c_ready = sem("tanh_c_ready")
        h_hi_ready = sem("h_hi_ready")
        h_full_ready = sem("h_full_ready")
        h_lo_ready = sem("h_lo_ready")
        hT_hi_in_psum = sem("hT_hi_in_psum")
        hT_lo_in_psum = sem("hT_lo_in_psum")
        hT_hi_ready = sem("hT_hi_ready")
        hT_lo_ready = sem("hT_lo_ready")
        out_ready = sem("out_ready")

        block = ctx.enter_context(nc.Block())

        @block.sync
        def _(sp):
            def load(slot, t0):
                for j in range(J):
                    dst = x_ring[j * N:(j + 1) * N, slot * CHUNK * P:(slot + 1) * CHUNK * P]
                    sp.dma_start(dst.rearrange("n (t f) -> n t f", f=P),
                                 x_v[j][:, bass.ds(t0, CHUNK), :]).then_inc(x_loaded, 16)

            def store(slot, t0):
                for j in range(J):
                    src = x_ring[j * N:(j + 1) * N, slot * CHUNK * P:(slot + 1) * CHUNK * P]
                    sp.dma_start(out_v[j][:, bass.ds(t0, CHUNK), :],
                                 src.rearrange("n (t f) -> n t f", f=P)).then_inc(out_stored, 16)

            load(0, 0)
            for k in range(J):
                sp.dma_start(w_raw[:, k, :], w_v[k]).then_inc(w_loaded[k], 16)
            for k in range(J, 2 * J):
                sp.dma_start(w_raw[:, k, :], w_v[k]).then_inc(w_loaded[k], 16)
            for c in range(1, SLOTS - 1):
                sp.wait_ge(x_loaded, 16 * J * c)
                load(c, c * CHUNK)

            def turn(c, slot, stores_before, loads_ahead):
                if loads_ahead:
                    if stores_before:
                        sp.wait_ge(out_stored, c * (16 * J))
                    sp.wait_ge(x_loaded, (c + (SLOTS - 1)) * (16 * J))
                    load((slot + SLOTS - 1) % SLOTS, (c + (SLOTS - 1)) * CHUNK)
                sp.wait_ge(out_ready, (c + 1) * CHUNK)
                store(slot, c * CHUNK)

            for c in range(SLOTS):
                turn(c, c, c > 0, True)
            with sp.Fori(1, CHUNKS // SLOTS - 1) as r:
                for slot in range(SLOTS):
                    turn(r * SLOTS + slot, slot, True, True)
            for slot in range(SLOTS):
                turn(CHUNKS - SLOTS + slot, slot, True, slot == 0)
            sp.wait_ge(out_stored, CHUNKS * 16 * J)

        @block.gpsimd
        def _(pool):
            for j in range(J):
                src = bias.rearrange("(o g f) -> o g f", o=1, g=GATES)[:, :, j * P:(j + 1) * P]
                pool.dma_start(bias_raw[j * N:(j + 1) * N, :].rearrange("n (g f) -> n g f", g=GATES),
                               src.broadcast_to([N, GATES, P])).then_inc(small_loaded, 16)
                pool.dma_start(h0_raw[j * N:(j + 1) * N, :],
                               h0[:, j * P:(j + 1) * P]).then_inc(small_loaded, 16)
            nc.gpsimd.memset(ident[:, :], 0.0).then_inc(ident_zeroed, 1)
            pool.wait_ge(ident_zeroed, 1)
            nc.gpsimd.affine_select(out=ident[:, :], in_=ident[:, :], compare_op=ALU.not_equal, fill=1.0,
                                    base=0, pattern=[[-1, P]], channel_multiplier=1).then_inc(ident_ready, 1)

        @block.tensor
        def _(pe):
            def pack(t_parity, part, k, stationary, w, last=False):
                for j in range(J):
                    mm = nc.tensor.matmul(gates[t_parity][j * N:(j + 1) * N, :],
                                          stationary[:, k * N:(k + 1) * N], w[:, part, k, j, :],
                                          start=False, stop=last, skip_group_check=True)
                return mm

            def x_packs(parity):
                x_hi, x_lo = xT[:, parity, 0, :], xT[:, parity, 1, :]
                return ([(x_hi, w_hi, k) for k in range(J)] + [(x_hi, w_lo, k) for k in range(J)]
                        + [(x_lo, w_hi, k) for k in range(J)])

            def x_project(parity, some):
                for stationary, w, k in x_packs(parity)[some]:
                    pack(parity, 0, k, stationary, w)

            def transpose_x(t, parity):
                pe.wait_ge(x_lo_ready, t + 1)
                nc.tensor.transpose(xT_ps[parity][:, 0:P], x_parts[:, parity, 0, :], ident[:, :])
                nc.tensor.transpose(xT_ps[parity][:, P:2 * P], x_parts[:, parity, 1, :],
                                    ident[:, :]).then_inc(xT_in_psum, 1)

            def transpose_h(ready, part, to, done, count):
                pe.wait_ge(ready, count)
                nc.tensor.transpose(to[:, :], part[:, :], ident[:, :]).then_inc(done, 1)

            def step(t, parity, more=True):
                pe.wait_ge(hT_hi_ready, t + 1)
                for k in range(J):
                    pack(parity, 1, k, hT_hi, w_hi)
                if more:
                    transpose_x(t + 1, 1 - parity)
                for k in range(J):
                    pack(parity, 1, k, hT_hi, w_lo)
                pe.wait_ge(hT_lo_ready, t + 1)
                for k in range(J):
                    mm = pack(parity, 1, k, hT_lo, w_hi, last=(k == J - 1))
                mm.then_inc(gates_ready, 1)
                if more:
                    pe.wait_ge(seeded, t + 2)
                    pe.wait_ge(xT_ready, t + 2)
                    x_project(1 - parity, slice(0, HEAD))
                    transpose_h(h_hi_ready, h_hi, hT_hi_ps, hT_hi_in_psum, t + 2)
                    x_project(1 - parity, slice(HEAD, None))
                    transpose_h(h_lo_ready, h_lo, hT_lo_ps, hT_lo_in_psum, t + 2)

            pe.wait_ge(ident_ready, 1)
            transpose_x(0, 0)
            transpose_h(h_hi_ready, h_hi, hT_hi_ps, hT_hi_in_psum, 1)
            transpose_h(h_lo_ready, h_lo, hT_lo_ps, hT_lo_in_psum, 1)
            pe.wait_ge(w_hi_ready, 1)
            for p in range(2):
                mm = nc.tensor.matmul(gates[p][:, :], ident[:, :], w_hi[:, 0, 0, 0, :], start=True, stop=True)
            mm.then_inc(banks_open, 1)
            pe.wait_ge(seeded, 1)
            pe.wait_ge(xT_ready, 1)
            pe.wait_ge(w_lo_ready, J)
            x_project(0, slice(0, None))
            pe.wait_ge(w_lo_ready, 2 * J)
            with pe.Fori(0, T - 2, 2) as t:
                step(t, 0)
                step(t + 1, 1)
            step(T - 2, 0)
            step(T - 1, 1, more=False)

        @block.scalar
        def _(act):
            def seed(parity):
                nc.scalar.activation(gates[parity][:, :], bias_sc[:, :], ACT.Copy).then_inc(seeded, 1)

            def evacuate_x(t, parity):
                act.wait_ge(xT_in_psum, t + 1)
                nc.scalar.activation(xT[:, parity, :, :].rearrange("p a b -> p (a b)"), xT_ps[parity][:, :],
                                     ACT.Copy).then_inc(xT_ready, 1)

            def evacuate_h(count):
                act.wait_ge(hT_hi_in_psum, count)
                nc.scalar.activation(hT_hi[:, :], hT_hi_ps[:, :], ACT.Copy).then_inc(hT_hi_ready, 1)

            def step(t, parity, more=True, seeds=True):
                if more:
                    evacuate_x(t + 1, 1 - parity)
                act.wait_ge(gates_ready, t + 1)
                bank = gates[parity]
                nc.scalar.activation(g_c[:, 0:P], bank[:, 3 * P:4 * P], ACT.Tanh, scale=UNSCALE)
                nc.scalar.activation(i_f[:, :], bank[:, 0:2 * P], ACT.Sigmoid,
                                     scale=UNSCALE).then_inc(ifg_ready, 1)
                nc.scalar.activation(o_gate[:, :], bank[:, 2 * P:3 * P], ACT.Sigmoid,
                                     scale=UNSCALE).then_inc(o_ready, 1)
                act.wait_ge(c_ready, t + 1)
                nc.scalar.activation(tanh_c[:, :], g_c[:, P:2 * P], ACT.Tanh).then_inc(tanh_c_ready, 1)
                if more:
                    evacuate_h(t + 2)
                if seeds:
                    seed(parity)

            act.preload_act_table_set("sigmoid_and_others")
            for n in range(2 * J):
                act.wait_ge(w_loaded[n], 16)
                src = w_raw[:, n, :].rearrange("p (g j f) -> p j g f", g=GATES, j=J)
                dst = w_hi[:, n // J, n % J, :, :].rearrange("p j (g f) -> p j g f", g=GATES)
                for j in range(J):
                    a = nc.scalar.activation(dst[:, j, :, :], src[:, j, :, :], ACT.Copy, scale=WSCALE)
                a.then_inc(w_hi_ready, 1)
                if n == J - 1:
                    act.wait_ge(small_loaded, 2 * 16 * J)
                    nc.scalar.activation(bias_sc[:, :], bias_raw[:, :], ACT.Copy,
                                         scale=WSCALE).then_inc(bias_ready, 1)
                    act.wait_ge(bias_ready, 1)
                    act.wait_ge(banks_open, 1)
                    seed(0)
                    seed(1)
                    evacuate_x(0, 0)
            evacuate_h(1)
            with act.Fori(0, T - 2, 2) as t:
                step(t, 0)
                step(t + 1, 1)
            step(T - 2, 0, seeds=False)
            step(T - 1, 1, more=False, seeds=False)

        @block.vector
        def _(dve):
            def split_x(t, parity):
                at = x_ring[:, bass.ds((t % RING) * P, P)]
                nc.vector.tensor_copy(x_parts[:, parity, 0, :], at).then_inc(x_hi_ready, 1)
                dve.wait_ge(x_hi_ready, t + 1)
                nc.vector.tensor_tensor(x_parts[:, parity, 1, :], at, x_parts[:, parity, 0, :],
                                        ALU.subtract).then_inc(x_lo_ready, 1)

            def evacuate_h(count):
                dve.wait_ge(hT_lo_in_psum, count)
                nc.vector.tensor_copy(hT_lo[:, :], hT_lo_ps[:, :]).then_inc(hT_lo_ready, 1)

            def step(t, parity, split_chunk=None, more=True, split=True):
                dve.wait_ge(ifg_ready, t + 1)
                nc.vector.tensor_tensor(prods[:, :], i_f[:, :], g_c[:, :], ALU.mult).then_inc(prods_ready, 1)
                dve.wait_ge(prods_ready, t + 1)
                nc.vector.tensor_tensor(g_c[:, P:2 * P], prods[:, 0:P], prods[:, P:2 * P],
                                        ALU.add).then_inc(c_ready, 1)
                dve.wait_ge(o_ready, t + 1)
                dve.wait_ge(tanh_c_ready, t + 1)
                if more:
                    nc.vector.tensor_tensor(h_hi[:, :], o_gate[:, :], tanh_c[:, :],
                                            ALU.mult).then_inc(h_hi_ready, 1)
                nc.vector.tensor_tensor(h_full[:, :], o_gate[:, :], tanh_c[:, :],
                                        ALU.mult).then_inc(h_full_ready, 1)
                dve.wait_ge(h_full_ready, t + 1)
                if more:
                    dve.wait_ge(h_hi_ready, t + 2)
                    nc.vector.tensor_tensor(h_lo[:, :], h_full[:, :], h_hi[:, :],
                                            ALU.subtract).then_inc(h_lo_ready, 1)
                    evacuate_h(t + 2)
                if split:
                    split_x(t + 2, parity)
                at = x_ring[:, bass.ds((t % RING) * P, P)]
                nc.vector.tensor_tensor(at, at, h_full[:, :], ALU.add).then_inc(out_ready, 1)

            nc.vector.memset(g_c[:, P:2 * P], 0.0).then_inc(c_zeroed, 1)
            dve.wait_ge(x_loaded, 16 * J)
            split_x(0, 0)
            split_x(1, 1)
            dve.wait_ge(small_loaded, 2 * 16 * J)
            nc.vector.tensor_copy(h_hi[:, :], h0_raw[:, :]).then_inc(h_hi_ready, 1)
            dve.wait_ge(h_hi_ready, 1)
            nc.vector.tensor_tensor(h_lo[:, :], h0_raw[:, :], h_hi[:, :], ALU.subtract).then_inc(h_lo_ready, 1)
            evacuate_h(1)
            for n in range(2 * J):
                dve.wait_ge(w_hi_ready, n + 1)
                src = w_raw[:, n, :].rearrange("p (g j f) -> p j g f", g=GATES, j=J)
                hi = w_hi[:, n // J, n % J, :, :].rearrange("p j (g f) -> p j g f", g=GATES)
                lo = w_lo[:, n // J, n % J, :, :].rearrange("p j (g f) -> p j g f", g=GATES)
                for j in range(J):
                    s = nc.vector.scalar_tensor_tensor(out=lo[:, j, :, :], in0=src[:, j, :, :], scalar=WSCALE,
                                                       in1=hi[:, j, :, :], op0=ALU.mult, op1=ALU.subtract)
                s.then_inc(w_lo_ready, 1)
            dve.wait_ge(c_zeroed, 1)
            with dve.Fori(0, T - CHUNK, CHUNK) as t0:
                with dve.Fori(0, CHUNK - 2, 2) as s:
                    step(t0 + s, 0)
                    step(t0 + s + 1, 1)
                dve.wait_ge(x_loaded, (t0 + 2 * CHUNK) * J)
                step(t0 + CHUNK - 2, 0)
                step(t0 + CHUNK - 1, 1)
            with dve.Fori(T - CHUNK, T - 2, 2) as t:
                step(t, 0)
                step(t + 1, 1)
            step(T - 2, 0, split=False)
            step(T - 1, 1, more=False, split=False)


_INS = ['x', 'cond_1024', 'L0_cond_Wx', 'L0_cond_Wh', 'L0_cond_b']


def kernel(**inputs):
    import numpy as _np
    import concourse.bacc as _bacc
    from concourse import mybir as _mybir
    from concourse.bass_utils import run_bass_kernel_spmd as _run

    nc = _bacc.Bacc("TRN2", target_bir_lowering=False, num_devices=1)
    arrays, args = {}, []
    for name in _INS:
        a = _np.ascontiguousarray(inputs[name])
        arrays[f"in_{name}_dram"] = a
        args.append(nc.dram_tensor(f"in_{name}_dram", a.shape, _mybir.dt.from_np(a.dtype), kind="ExternalInput").ap())
    o = nc.dram_tensor("out_0_dram", inputs['x'].shape, _mybir.dt.float32, kind="ExternalOutput").ap()
    lstm_residual(nc, *args, o)
    r = _run(nc, [arrays], core_ids=[0])
    return r.results[0]["out_0_dram"]
```

```python
from contextlib import ExitStack

import concourse.bass as bass
from concourse import mybir

ALU = mybir.AluOpType
ACT = mybir.ActivationFunctionType
F32 = mybir.dt.float32
F16 = mybir.dt.float16

P = 128
GATES = 4
WSCALE = 64.0
BODY = 8
SLOTS = 4
ITEM_AHEAD = 6
XT_AHEAD = 10
SPLIT_AHEAD = 11
HEAD = 10


def lstm_residual(nc, x, h0, w_x, w_h, bias, out):
    N, T, D = x.shape
    H = h0.shape[1]
    J = D // P
    assert D == H and J * N == P and w_x.shape[1] == GATES * H
    G = GATES * P
    GROUP = P // N
    assert GROUP == J and BODY == 2 * GROUP
    RING = BODY * SLOTS
    CHUNKS = T // BODY
    TAIL = 2 * BODY
    assert T % BODY == 0 and T >= 2 * RING and SPLIT_AHEAD < TAIL
    X_DMA = 16 * J
    MOVE_DMA = 16 * GROUP
    UNSCALE = 1.0 / WSCALE

    x_v = [x[:, :, j * P:(j + 1) * P] for j in range(J)]
    out_v = [out[:, :, j * P:(j + 1) * P] for j in range(J)]
    w_v = [w[k * P:(k + 1) * P, :] for w in (w_x, w_h) for k in range(J)]

    with ExitStack() as ctx:
        def sb(name, shape, dt):
            return ctx.enter_context(nc.sbuf_tensor(name, shape, dt))

        def psum(name, shape, dt):
            return ctx.enter_context(nc.psum_tensor(name, shape, dt))

        def sem(name):
            return ctx.enter_context(nc.semaphore(name))

        w_hi = sb("w_hi", [P, 2, J, J, G], F16)
        w_lo = sb("w_lo", [P, 2, J, J, G], F16)
        w_raw = sb("w_raw", [P, J, GATES * H], F32)
        bias_raw = sb("bias_raw", [P, J, G], F32)
        bias_sc = sb("bias_sc", [P, J, G], F32)
        ident = sb("ident", [P, P], F16)
        x_ring = sb("x_ring", [P, RING * P], F32)
        h0_raw = sb("h0_raw", [P, P], F32)
        x_parts = sb("x_parts", [P, 2, 2, P], F16)
        xT = sb("xT", [P, 2, 2, J, GROUP, N], F16)
        xw_stage = sb("xw_stage", [P, 2, G], F32)
        xw = sb("xw", [P, 2, GROUP, G], F32)
        h_hi = sb("h_hi", [P, P], F16)
        h_lo = sb("h_lo", [P, P], F16)
        h_full = sb("h_full", [P, P], F32)
        hT_hi = sb("hT_hi", [P, P], F16)
        hT_lo = sb("hT_lo", [P, P], F16)
        i_f = sb("i_f", [P, 2 * P], F32)
        o_gate = sb("o_gate", [P, P], F32)
        g_c = sb("g_c", [P, 2 * P], F32)
        prods = sb("prods", [P, 2 * P], F32)
        tanh_c = sb("tanh_c", [P, P], F32)

        gates = [psum(f"gates{p}", [P, G], F32) for p in range(2)]
        xw_ps = [psum(f"xw_ps{p}", [P, G], F32) for p in range(2)]
        xT_ps = [psum(f"xT_ps{p}", [P, 2 * P], F16) for p in range(2)]
        hT_hi_ps = psum("hT_hi_ps", [P, P], F16)
        hT_lo_ps = psum("hT_lo_ps", [P, P], F16)

        w_loaded = [sem(f"w_loaded{n}") for n in range(2 * J)]
        bias_loaded = sem("bias_loaded")
        h0_loaded = sem("h0_loaded")
        ident_zeroed = sem("ident_zeroed")
        ident_ready = sem("ident_ready")
        w_hi_ready = sem("w_hi_ready")
        w_lo_ready = sem("w_lo_ready")
        bias_ready = sem("bias_ready")
        banks_open = sem("banks_open")
        c_zeroed = sem("c_zeroed")
        x_loaded = sem("x_loaded")
        out_stored = sem("out_stored")
        x_hi_ready = sem("x_hi_ready")
        x_lo_ready = sem("x_lo_ready")
        xT_in_psum = sem("xT_in_psum")
        xT_ready = sem("xT_ready")
        xw_in_psum = sem("xw_in_psum")
        xw_staged = sem("xw_staged")
        xw_moved = [sem(f"xw_moved{p}") for p in range(2)]
        seeded = sem("seeded")
        gates_ready = sem("gates_ready")
        ifg_ready = sem("ifg_ready")
        o_ready = sem("o_ready")
        prods_ready = sem("prods_ready")
        c_ready = sem("c_ready")
        tanh_c_ready = sem("tanh_c_ready")
        h_hi_ready = sem("h_hi_ready")
        h_full_ready = sem("h_full_ready")
        h_lo_ready = sem("h_lo_ready")
        hT_hi_in_psum = sem("hT_hi_in_psum")
        hT_lo_in_psum = sem("hT_lo_in_psum")
        hT_hi_ready = sem("hT_hi_ready")
        hT_lo_ready = sem("hT_lo_ready")
        out_ready = sem("out_ready")

        block = ctx.enter_context(nc.Block())

        def steps(eng, step):
            with eng.Fori(0, T - TAIL, BODY) as t0:
                for s in range(BODY):
                    step(t0 + s, s, TAIL)
            for t in range(T - TAIL, T):
                step(t, t % BODY, T - 1 - t)

        @block.sync
        def _(sp):
            def in_ring(j, slot):
                rows = x_ring[j * N:(j + 1) * N, bass.ds(slot * (BODY * P), BODY * P)]
                return rows.rearrange("n (t f) -> n t f", f=P)

            def load(slot, t0):
                for j in range(J):
                    sp.dma_start(in_ring(j, slot), x_v[j][:, bass.ds(t0, BODY), :]).then_inc(x_loaded, 16)

            def store(slot, t0):
                for j in range(J):
                    sp.dma_start(out_v[j][:, bass.ds(t0, BODY), :], in_ring(j, slot)).then_inc(out_stored, 16)

            def move(m, m8):
                j, group = m8 % GROUP, m8 // GROUP
                sp.wait_ge(xw_staged, m + 1)
                for r in range(GROUP):
                    sp.dma_start(xw[j * N:(j + 1) * N, group, r, :],
                                 xw_stage[r * N:(r + 1) * N, m8 % 2, :]).then_inc(xw_moved[m8 % 2], 16)

            def chunk(c, first=False, moves=BODY, loads=True):
                slot = (c + (SLOTS - 1)) % SLOTS
                t_in, t_out = (c + (SLOTS - 1)) * BODY, (c - 1) * BODY
                if not isinstance(c, int):
                    slot, t_in, t_out = sp.snap(slot), sp.snap(t_in), sp.snap(t_out)
                for s in range(BODY):
                    if s < moves:
                        move(c * BODY + s + ITEM_AHEAD, (s + ITEM_AHEAD) % BODY)
                    if s == 3 and not first:
                        sp.wait_ge(out_ready, c * BODY)
                        store(slot, t_out)
                    if s == 6 and loads:
                        if not first:
                            sp.wait_ge(out_stored, c * X_DMA)
                        load(slot, t_in)

            load(0, 0)
            for k in range(J):
                sp.dma_start(w_raw[:, k, :], w_v[k]).then_inc(w_loaded[k], 16)
            sp.wait_ge(x_loaded, X_DMA)
            load(1, BODY)
            for k in range(J):
                sp.wait_ge(w_lo_ready, k + 1)
                sp.dma_start(w_raw[:, k, :], w_v[J + k]).then_inc(w_loaded[J + k], 16)
            sp.wait_ge(x_loaded, 2 * X_DMA)
            load(2, 2 * BODY)
            for m in range(ITEM_AHEAD):
                move(m, m)
            chunk(0, first=True)
            with sp.Fori(1, CHUNKS - (SLOTS - 1)) as c:
                chunk(c)
            for c in range(CHUNKS - (SLOTS - 1), CHUNKS - 1):
                chunk(c, loads=False)
            chunk(CHUNKS - 1, moves=BODY - ITEM_AHEAD, loads=False)
            sp.wait_ge(out_ready, T)
            store((CHUNKS - 1) % SLOTS, T - BODY)
            sp.wait_ge(out_stored, CHUNKS * X_DMA)

        @block.gpsimd
        def _(pool):
            for j in range(J):
                pool.dma_start(h0_raw[j * N:(j + 1) * N, :], h0[:, j * P:(j + 1) * P]).then_inc(h0_loaded, 16)
            for j in range(J):
                src = bias.rearrange("(o g f) -> o g f", o=1, g=GATES)[:, :, j * P:(j + 1) * P]
                pool.dma_start(bias_raw[:, j, :].rearrange("p (g f) -> p g f", g=GATES),
                               src.broadcast_to([P, GATES, P])).then_inc(bias_loaded, 16)
            nc.gpsimd.memset(ident[:, :], 0.0).then_inc(ident_zeroed, 1)
            pool.wait_ge(ident_zeroed, 1)
            nc.gpsimd.affine_select(out=ident[:, :], in_=ident[:, :], compare_op=ALU.not_equal, fill=1.0,
                                    base=0, pattern=[[-1, P]], channel_multiplier=1).then_inc(ident_ready, 1)

        @block.tensor
        def _(pe):
            def recur(parity, k, stationary, w, last=False):
                for j in range(J):
                    mm = nc.tensor.matmul(gates[parity][j * N:(j + 1) * N, :], stationary[:, k * N:(k + 1) * N],
                                          w[:, 1, k, j, :], start=False, stop=last, skip_group_check=True)
                return mm

            def project(m8, some):
                j, group = m8 % GROUP, m8 // GROUP
                products = [(k, 0, w_hi) for k in range(J)] + [(k, 0, w_lo) for k in range(J)] \
                    + [(k, 1, w_hi) for k in range(J)]
                for n in range(len(products))[some]:
                    k, part, w = products[n]
                    mm = nc.tensor.matmul(xw_ps[m8 % 2][:, :],
                                          xT[:, group, part, k, :, :].rearrange("f r n -> f (r n)"),
                                          w[:, 0, k, j, :], start=(n == 0), stop=(n == len(products) - 1))
                return mm


            def transpose_x(t, s):
                pe.wait_ge(x_lo_ready, t + 1)
                to = xT_ps[s % 2]
                nc.tensor.transpose(to[:, 0:P], x_parts[:, s % 2, 0, :], ident[:, :])
                nc.tensor.transpose(to[:, P:2 * P], x_parts[:, s % 2, 1, :], ident[:, :]).then_inc(xT_in_psum, 1)

            def transpose_h(ready, part, to, done, count):
                pe.wait_ge(ready, count)
                nc.tensor.transpose(to[:, :], part[:, :], ident[:, :]).then_inc(done, 1)

            def step(t, s, left):
                now = t + 1 if isinstance(t, int) else pe.snap(t + 1)
                pe.wait_ge(seeded, now)
                pe.wait_ge(hT_hi_ready, now)
                for k in range(J):
                    recur(s % 2, k, hT_hi, w_hi)
                for k in range(J):
                    recur(s % 2, k, hT_hi, w_lo)
                pe.wait_ge(hT_lo_ready, now)
                for k in range(J):
                    mm = recur(s % 2, k, hT_lo, w_hi, last=(k == J - 1))
                mm.then_inc(gates_ready, 1)
                m8 = (s + ITEM_AHEAD) % BODY
                if left >= XT_AHEAD:
                    transpose_x(t + XT_AHEAD, s + XT_AHEAD)
                if left >= ITEM_AHEAD:
                    if m8 % GROUP == 0:
                        pe.wait_ge(xT_ready, t + (ITEM_AHEAD + GROUP))
                    project(m8, slice(0, HEAD))
                if left:
                    transpose_h(h_hi_ready, h_hi, hT_hi_ps, hT_hi_in_psum, t + 2)
                if left >= ITEM_AHEAD:
                    project(m8, slice(HEAD, None)).then_inc(xw_in_psum, 1)
                if left:
                    transpose_h(h_lo_ready, h_lo, hT_lo_ps, hT_lo_in_psum, t + 2)

            pe.wait_ge(ident_ready, 1)
            transpose_h(h_hi_ready, h_hi, hT_hi_ps, hT_hi_in_psum, 1)
            transpose_h(h_lo_ready, h_lo, hT_lo_ps, hT_lo_in_psum, 1)
            def first_transpose(t):
                if t >= 2:
                    pe.wait_ge(xT_ready, t - 1)
                transpose_x(t, t)

            for t in range(2 * GROUP):
                first_transpose(t)
            pe.wait_ge(w_hi_ready, 1)
            for p in range(2):
                mm = nc.tensor.matmul(gates[p][:, :], ident[:, :], w_hi[:, 0, 0, 0, :], start=True, stop=True)
            mm.then_inc(banks_open, 1)
            pe.wait_ge(w_lo_ready, J)
            for m in range(ITEM_AHEAD):
                if m % GROUP == 0:
                    pe.wait_ge(xT_ready, m + GROUP)
                if m >= 2:
                    pe.wait_ge(xw_staged, m - 1)
                project(m, slice(None)).then_inc(xw_in_psum, 1)
                if m + 1 >= GROUP and m + 1 + GROUP < XT_AHEAD:
                    first_transpose(m + 1 + GROUP)
            pe.wait_ge(w_lo_ready, 2 * J)
            steps(pe, step)

        @block.scalar
        def _(act):
            def seed(t, s):
                if s % GROUP == 0:
                    for p in range(2):
                        act.wait_ge(xw_moved[p], (t + GROUP) * (MOVE_DMA // 2))
                nc.scalar.activation(gates[s % 2][:, :], xw[:, s // GROUP, s % GROUP, :],
                                     ACT.Copy).then_inc(seeded, 1)

            def evacuate_x(t, s):
                act.wait_ge(xT_in_psum, t + 1)
                nc.scalar.activation(xT[:, s // GROUP, :, :, s % GROUP, :],
                                     xT_ps[s % 2][:, :].rearrange("f (a j n) -> f a j n", a=2, j=J),
                                     ACT.Copy).then_inc(xT_ready, 1)

            def evacuate_h(count):
                act.wait_ge(hT_hi_in_psum, count)
                nc.scalar.activation(hT_hi[:, :], hT_hi_ps[:, :], ACT.Copy).then_inc(hT_hi_ready, 1)

            def step(t, s, left):
                act.wait_ge(gates_ready, t + 1)
                bank = gates[s % 2]
                nc.scalar.activation(g_c[:, 0:P], bank[:, 3 * P:4 * P], ACT.Tanh, scale=UNSCALE)
                nc.scalar.activation(i_f[:, :], bank[:, 0:2 * P], ACT.Sigmoid,
                                     scale=UNSCALE).then_inc(ifg_ready, 1)
                nc.scalar.activation(o_gate[:, :], bank[:, 2 * P:3 * P], ACT.Sigmoid,
                                     scale=UNSCALE).then_inc(o_ready, 1)
                act.wait_ge(c_ready, t + 1)
                nc.scalar.activation(tanh_c[:, :], g_c[:, P:2 * P], ACT.Tanh).then_inc(tanh_c_ready, 1)
                if left:
                    evacuate_h(t + 2)
                if left >= 2:
                    seed(t + 2, (s + 2) % BODY)
                if left >= XT_AHEAD:
                    evacuate_x(t + XT_AHEAD, (s + XT_AHEAD) % BODY)

            def split_hi(n):
                act.wait_ge(w_loaded[n], 16)
                src = w_raw[:, n % J, :].rearrange("p (g j f) -> p j g f", g=GATES, j=J)
                dst = w_hi[:, n // J, n % J, :, :].rearrange("p j (g f) -> p j g f", g=GATES)
                for j in range(J):
                    a = nc.scalar.activation(dst[:, j, :, :], src[:, j, :, :], ACT.Copy, scale=WSCALE)
                a.then_inc(w_hi_ready, 1)

            act.preload_act_table_set("sigmoid_and_others")
            evacuate_h(1)
            for t in range(BODY):
                evacuate_x(t, t)
            for n in range(J):
                split_hi(n)
            act.wait_ge(bias_loaded, 16 * J)
            nc.scalar.activation(bias_sc[:, :, :], bias_raw[:, :, :], ACT.Copy, scale=WSCALE).then_inc(bias_ready, 1)
            split_hi(J)
            split_hi(J + 1)
            for t in range(BODY, XT_AHEAD):
                evacuate_x(t, t % BODY)
            for n in range(J + 2, 2 * J):
                split_hi(n)
            act.wait_ge(banks_open, 1)
            seed(0, 0)
            seed(1, 1)
            steps(act, step)

        @block.vector
        def _(dve):
            def in_ring(t):
                return x_ring[:, bass.ds((t % RING) * P, P)]

            def split_x(t, s):
                nc.vector.tensor_copy(x_parts[:, s % 2, 0, :], in_ring(t)).then_inc(x_hi_ready, 1)
                dve.wait_ge(x_hi_ready, t + 1)
                nc.vector.tensor_tensor(x_parts[:, s % 2, 1, :], in_ring(t), x_parts[:, s % 2, 0, :],
                                        ALU.subtract).then_inc(x_lo_ready, 1)

            def stage(m, m8):
                dve.wait_ge(xw_in_psum, m + 1)
                if not isinstance(m, int) or m >= 2:
                    dve.wait_ge(xw_moved[m8 % 2], (m - m8 % 2) * (MOVE_DMA // 2))
                nc.vector.tensor_tensor(xw_stage[:, m8 % 2, :], xw_ps[m8 % 2][:, :], bias_sc[:, m8 % GROUP, :],
                                        ALU.add).then_inc(xw_staged, 1)

            def evacuate_h(count):
                dve.wait_ge(hT_lo_in_psum, count)
                nc.vector.tensor_copy(hT_lo[:, :], hT_lo_ps[:, :]).then_inc(hT_lo_ready, 1)

            def step(t, s, left):
                dve.wait_ge(ifg_ready, t + 1)
                nc.vector.tensor_tensor(prods[:, :], i_f[:, :], g_c[:, :], ALU.mult).then_inc(prods_ready, 1)
                dve.wait_ge(prods_ready, t + 1)
                nc.vector.tensor_tensor(g_c[:, P:2 * P], prods[:, 0:P], prods[:, P:2 * P],
                                        ALU.add).then_inc(c_ready, 1)
                dve.wait_ge(o_ready, t + 1)
                dve.wait_ge(tanh_c_ready, t + 1)
                if left:
                    nc.vector.tensor_tensor(h_hi[:, :], o_gate[:, :], tanh_c[:, :],
                                            ALU.mult).then_inc(h_hi_ready, 1)
                nc.vector.tensor_tensor(h_full[:, :], o_gate[:, :], tanh_c[:, :],
                                        ALU.mult).then_inc(h_full_ready, 1)
                dve.wait_ge(h_full_ready, t + 1)
                if left:
                    dve.wait_ge(h_hi_ready, t + 2)
                    nc.vector.tensor_tensor(h_lo[:, :], h_full[:, :], h_hi[:, :],
                                            ALU.subtract).then_inc(h_lo_ready, 1)
                    evacuate_h(t + 2)
                if left >= ITEM_AHEAD:
                    stage(t + ITEM_AHEAD, (s + ITEM_AHEAD) % BODY)
                if left >= SPLIT_AHEAD:
                    if (s + SPLIT_AHEAD) % BODY == 0:
                        dve.wait_ge(x_loaded, (t + (SPLIT_AHEAD + BODY)) * (X_DMA // BODY))
                    split_x(t + SPLIT_AHEAD, s + SPLIT_AHEAD)
                nc.vector.tensor_tensor(in_ring(t), in_ring(t), h_full[:, :], ALU.add).then_inc(out_ready, 1)

            def split_lo(n):
                dve.wait_ge(w_hi_ready, n + 1)
                src = w_raw[:, n % J, :].rearrange("p (g j f) -> p j g f", g=GATES, j=J)
                hi = w_hi[:, n // J, n % J, :, :].rearrange("p j (g f) -> p j g f", g=GATES)
                lo = w_lo[:, n // J, n % J, :, :].rearrange("p j (g f) -> p j g f", g=GATES)
                for j in range(J):
                    v = nc.vector.scalar_tensor_tensor(out=lo[:, j, :, :], in0=src[:, j, :, :], scalar=WSCALE,
                                                       in1=hi[:, j, :, :], op0=ALU.mult, op1=ALU.subtract)
                v.then_inc(w_lo_ready, 1)

            def split_prologue(t):
                if t >= 2:
                    dve.wait_ge(xT_in_psum, t - 1)
                split_x(t, t)

            nc.vector.memset(g_c[:, P:2 * P], 0.0).then_inc(c_zeroed, 1)
            dve.wait_ge(h0_loaded, 16 * J)
            nc.vector.tensor_copy(h_hi[:, :], h0_raw[:, :]).then_inc(h_hi_ready, 1)
            dve.wait_ge(h_hi_ready, 1)
            nc.vector.tensor_tensor(h_lo[:, :], h0_raw[:, :], h_hi[:, :], ALU.subtract).then_inc(h_lo_ready, 1)
            evacuate_h(1)
            dve.wait_ge(x_loaded, X_DMA)
            for t in range(BODY):
                split_prologue(t)
            for n in range(J):
                split_lo(n)
            dve.wait_ge(x_loaded, 2 * X_DMA)
            for t in range(BODY, XT_AHEAD):
                split_prologue(t)
            dve.wait_ge(bias_ready, 1)
            for m in range(ITEM_AHEAD):
                stage(m, m)
                if m < J:
                    split_lo(J + m)
            for t in range(XT_AHEAD, SPLIT_AHEAD):
                split_prologue(t)
            dve.wait_ge(c_zeroed, 1)
            steps(dve, step)


_INS = ['x', 'cond_1024', 'L0_cond_Wx', 'L0_cond_Wh', 'L0_cond_b']


def kernel(**inputs):
    import numpy as _np
    import concourse.bacc as _bacc
    from concourse import mybir as _mybir
    from concourse.bass_utils import run_bass_kernel_spmd as _run

    nc = _bacc.Bacc("TRN2", target_bir_lowering=False, num_devices=1)
    arrays, args = {}, []
    for name in _INS:
        a = _np.ascontiguousarray(inputs[name])
        arrays[f"in_{name}_dram"] = a
        args.append(nc.dram_tensor(f"in_{name}_dram", a.shape, _mybir.dt.from_np(a.dtype), kind="ExternalInput").ap())
    o = nc.dram_tensor("out_0_dram", inputs['x'].shape, _mybir.dt.float32, kind="ExternalOutput").ap()
    lstm_residual(nc, *args, o)
    r = _run(nc, [arrays], core_ids=[0])
    return r.results[0]["out_0_dram"]
```

```python
from contextlib import ExitStack

import concourse.bass as bass
from concourse import mybir

ALU = mybir.AluOpType
ACT = mybir.ActivationFunctionType
F32 = mybir.dt.float32
F16 = mybir.dt.float16

P = 128
GATES = 4
WSCALE = 64.0
BODY = 8
SLOTS = 4
ITEM_AHEAD = 6
XT_AHEAD = 10


def lstm_residual(nc, x, h0, w_x, w_h, bias, out):
    N, T, D = x.shape
    H = h0.shape[1]
    J = D // P
    assert D == H and J * N == P and w_x.shape[1] == GATES * H
    G = GATES * P
    GROUP = P // N
    assert GROUP == J and BODY == 2 * GROUP
    RING = BODY * SLOTS
    CHUNKS = T // BODY
    TAIL = 2 * BODY
    assert T % BODY == 0 and T >= 2 * RING and XT_AHEAD < TAIL
    X_DMA = 16 * J
    MOVE_DMA = 16
    UNSCALE = 1.0 / WSCALE

    x_v = [x[:, :, j * P:(j + 1) * P] for j in range(J)]
    out_v = [out[:, :, j * P:(j + 1) * P] for j in range(J)]
    w_v = [w.rearrange("(j k e) g -> k j e g", j=J, k=J)[k] for w in (w_x, w_h) for k in range(J)]

    with ExitStack() as ctx:
        def sb(name, shape, dt):
            return ctx.enter_context(nc.sbuf_tensor(name, shape, dt))

        def psum(name, shape, dt):
            return ctx.enter_context(nc.psum_tensor(name, shape, dt))

        def sem(name):
            return ctx.enter_context(nc.semaphore(name))

        w_hi = sb("w_hi", [P, 2, J, J, G], F16)
        w_lo = sb("w_lo", [P, 2, J, J, G], F16)
        w_raw = sb("w_raw", [P, 2 * J, GATES * H], F32)
        bias_raw = sb("bias_raw", [P, J, G], F32)
        bias_sc = sb("bias_sc", [P, J, G], F32)
        x_ring = sb("x_ring", [P, RING * P], F32)
        h0_raw = sb("h0_raw", [P, P], F32)
        x_parts = sb("x_parts", [P, 2, P], F16)
        xT = sb("xT", [P, 2, 2, J, N, GROUP], F16)
        xw_stage = sb("xw_stage", [P, 2, G], F32)
        xw = sb("xw", [P, 2, GROUP, G], F32)
        h_hi = sb("h_hi", [P, P], F16)
        h_lo = sb("h_lo", [P, P], F16)
        h_full = sb("h_full", [P, P], F32)
        hT_hi = sb("hT_hi", [P, P], F16)
        hT_lo = sb("hT_lo", [P, P], F16)
        i_f = sb("i_f", [P, 2 * P], F32)
        g_gate = sb("g_gate", [P, P], F32)
        o_gate = sb("o_gate", [P, P], F32)
        c_state = sb("c_state", [P, P], F32)
        i_g = sb("i_g", [P, P], F32)
        f_c = sb("f_c", [P, P], F32)
        tanh_c = sb("tanh_c", [P, P], F32)

        gates = [psum(f"gates{p}", [P, G], F32) for p in range(2)]
        xw_ps = [psum(f"xw_ps{p}", [P, G], F32) for p in range(2)]

        w_loaded = [sem(f"w_loaded{n}") for n in range(2 * J)]
        bias_loaded = sem("bias_loaded")
        h0_loaded = sem("h0_loaded")
        w_hi_ready = sem("w_hi_ready")
        w_lo_ready = sem("w_lo_ready")
        bias_ready = sem("bias_ready")
        banks_open = sem("banks_open")
        c_zeroed = sem("c_zeroed")
        x_loaded = sem("x_loaded")
        out_stored = sem("out_stored")
        x_hi_ready = sem("x_hi_ready")
        x_lo_ready = sem("x_lo_ready")
        xT_ready = sem("xT_ready")
        xw_in_psum = sem("xw_in_psum")
        xw_staged = sem("xw_staged")
        xw_moved = [sem(f"xw_moved{p}") for p in range(2)]
        seeded = sem("seeded")
        gates_ready = sem("gates_ready")
        if_ready = sem("if_ready")
        g_ready = sem("g_ready")
        o_ready = sem("o_ready")
        i_g_ready = sem("i_g_ready")
        c_ready = sem("c_ready")
        tanh_c_ready = sem("tanh_c_ready")
        h_hi_ready = sem("h_hi_ready")
        h_full_ready = sem("h_full_ready")
        h_lo_ready = sem("h_lo_ready")
        hT_hi_ready = sem("hT_hi_ready")
        hT_lo_ready = sem("hT_lo_ready")
        out_ready = sem("out_ready")

        block = ctx.enter_context(nc.Block())

        def steps(engine, step):
            with nc.Fori(0, T - TAIL, BODY, engines=(engine,), hint_back_edge=True) as t0:
                for s in range(BODY):
                    step(t0 + s, s, TAIL)
            for t in range(T - TAIL, T):
                step(t, t % BODY, T - 1 - t)

        @block.sync
        def _(sp):
            def in_ring(j, slot):
                rows = x_ring[j * N:(j + 1) * N, bass.ds(slot * (BODY * P), BODY * P)]
                return rows.rearrange("n (t f) -> n t f", f=P)

            def load(slot, t0):
                for j in range(J):
                    sp.dma_start(in_ring(j, slot), x_v[j][:, bass.ds(t0, BODY), :]).then_inc(x_loaded, 16)

            def store(slot, t0):
                for j in range(J):
                    sp.dma_start(out_v[j][:, bass.ds(t0, BODY), :], in_ring(j, slot)).then_inc(out_stored, 16)

            def move(m, m8):
                j, group = m8 % GROUP, m8 // GROUP
                sp.wait_ge(xw_staged, m + 1)
                sp.dma_start(xw[j * N:(j + 1) * N, group, :, :], xw_stage[:, m8 % 2, :]
                             ).then_inc(xw_moved[m8 % 2], MOVE_DMA)

            def chunk(c, first=False, moves=BODY, loads=True):
                slot = (c + (SLOTS - 1)) % SLOTS
                t_in, t_out = (c + (SLOTS - 1)) * BODY, (c - 1) * BODY
                if not isinstance(c, int):
                    slot, t_in, t_out = sp.snap(slot), sp.snap(t_in), sp.snap(t_out)
                for s in range(BODY):
                    if s < moves:
                        move(c * BODY + s + ITEM_AHEAD, (s + ITEM_AHEAD) % BODY)
                    if s == 3 and not first:
                        sp.wait_ge(out_ready, c * BODY)
                        store(slot, t_out)
                    if s == BODY - 1 and loads:
                        if not first:
                            sp.wait_ge(out_stored, c * X_DMA)
                        load(slot, t_in)

            load(0, 0)
            for n in range(J):
                sp.dma_start(w_raw[:, n, :], w_v[n]).then_inc(w_loaded[n], 16)
            for j in range(J):
                src = bias.rearrange("(o g f) -> o g f", o=1, g=GATES)[:, :, j * P:(j + 1) * P]
                sp.dma_start(bias_raw[:, j, :].rearrange("p (g f) -> p g f", g=GATES),
                             src.broadcast_to([P, GATES, P])).then_inc(bias_loaded, 16)
            for n in range(J, 2 * J):
                sp.dma_start(w_raw[:, n, :], w_v[n]).then_inc(w_loaded[n], 16)
            sp.wait_ge(x_loaded, X_DMA)
            load(1, BODY)
            for m in range(ITEM_AHEAD):
                move(m, m)
            sp.wait_ge(x_loaded, 2 * X_DMA)
            load(2, 2 * BODY)
            chunk(0, first=True)
            with sp.Fori(1, CHUNKS - (SLOTS - 1)) as c:
                chunk(c)
            for c in range(CHUNKS - (SLOTS - 1), CHUNKS - 1):
                chunk(c, loads=False)
            chunk(CHUNKS - 1, moves=BODY - ITEM_AHEAD, loads=False)
            sp.wait_ge(out_ready, T)
            store((CHUNKS - 1) % SLOTS, T - BODY)
            sp.wait_ge(out_stored, CHUNKS * X_DMA)

        @block.tensor
        def _(pe):
            def recur(parity, k, stationary, w, last=False):
                for j in range(J):
                    mm = nc.tensor.matmul(gates[parity][j * N:(j + 1) * N, :], stationary[:, k * N:(k + 1) * N],
                                          w[:, 1, k, j, :], start=False, stop=last, skip_group_check=True)
                return mm

            def project(m8):
                j, group = m8 % GROUP, m8 // GROUP
                products = [(k, 0, w_hi) for k in range(J)] + [(k, 0, w_lo) for k in range(J)] \
                    + [(k, 1, w_hi) for k in range(J)]
                for n, (k, part, w) in enumerate(products):
                    mm = nc.tensor.matmul(xw_ps[m8 % 2][:, :],
                                          xT[:, group, part, k, :, :].rearrange("f n r -> f (n r)"),
                                          w[:, 0, k, j, :], start=(n == 0), stop=(n == len(products) - 1))
                return mm

            def step(t, s, left):
                now = t + 1 if isinstance(t, int) else pe.snap(t + 1)
                pe.wait_ge(seeded, now)
                pe.wait_ge(hT_hi_ready, now)
                for k in range(J):
                    recur(s % 2, k, hT_hi, w_hi)
                for k in range(J):
                    recur(s % 2, k, hT_hi, w_lo)
                pe.wait_ge(hT_lo_ready, now)
                for k in range(J):
                    mm = recur(s % 2, k, hT_lo, w_hi, last=(k == J - 1))
                mm.then_inc(gates_ready, 1)
                if left >= ITEM_AHEAD:
                    m8 = (s + ITEM_AHEAD) % BODY
                    if m8 % GROUP == 0:
                        pe.wait_ge(xT_ready, t + (ITEM_AHEAD + GROUP))
                    project(m8).then_inc(xw_in_psum, 1)

            pe.wait_ge(w_hi_ready, 1)
            for p in range(2):
                mm = nc.tensor.matmul(gates[p][:, :], w_hi[:, 0, 0, 0, 0:P], w_hi[:, 0, 0, 0, :],
                                      start=True, stop=True)
            mm.then_inc(banks_open, 1)
            pe.wait_ge(w_lo_ready, J)
            for m in range(ITEM_AHEAD):
                if m % GROUP == 0:
                    pe.wait_ge(xT_ready, m + GROUP)
                if m >= 2:
                    pe.wait_ge(xw_staged, m - 1)
                project(m).then_inc(xw_in_psum, 1)
            pe.wait_ge(w_lo_ready, 2 * J)
            pe.wait_ge(xw_staged, ITEM_AHEAD)
            steps(mybir.EngineType.PE, step)

        @block.scalar
        def _(act):
            def seed(t, s):
                if s % GROUP == 0:
                    for p in range(2):
                        act.wait_ge(xw_moved[p], (t + GROUP) * (MOVE_DMA // 2))
                nc.scalar.activation(gates[s % 2][:, :], xw[:, s // GROUP, s % GROUP, :],
                                     ACT.Copy).then_inc(seeded, 1)

            def step(t, s, left):
                act.wait_ge(gates_ready, t + 1)
                bank = gates[s % 2]
                nc.scalar.activation(i_f[:, :], bank[:, 0:2 * P], ACT.Sigmoid,
                                     scale=UNSCALE).then_inc(if_ready, 1)
                nc.scalar.activation(g_gate[:, :], bank[:, 3 * P:4 * P], ACT.Tanh,
                                     scale=UNSCALE).then_inc(g_ready, 1)
                nc.scalar.activation(o_gate[:, :], bank[:, 2 * P:3 * P], ACT.Sigmoid,
                                     scale=UNSCALE).then_inc(o_ready, 1)
                act.wait_ge(c_ready, t + 1)
                nc.scalar.activation(tanh_c[:, :], c_state[:, :], ACT.Tanh).then_inc(tanh_c_ready, 1)
                if left >= 2:
                    act.wait_ge(o_ready, t + 1)
                    seed(t + 2, (s + 2) % BODY)

            def split_hi(n):
                act.wait_ge(w_loaded[n], 16)
                src = w_raw[:, n, :].rearrange("p (g j f) -> p j g f", g=GATES, j=J)
                dst = w_hi[:, n // J, n % J, :, :].rearrange("p j (g f) -> p j g f", g=GATES)
                for j in range(J):
                    a = nc.scalar.activation(dst[:, j, :, :], src[:, j, :, :], ACT.Copy, scale=WSCALE)
                a.then_inc(w_hi_ready, 1)

            act.dma_start(h0_raw[:, :], h0.rearrange("n (j f) -> j n f", j=J)).then_inc(h0_loaded, 16)
            act.preload_act_table_set("sigmoid_and_others")
            for n in range(J):
                split_hi(n)
            act.wait_ge(bias_loaded, 16 * J)
            nc.scalar.activation(bias_sc[:, :, :], bias_raw[:, :, :], ACT.Copy, scale=WSCALE).then_inc(bias_ready, 1)
            for n in range(J, 2 * J):
                split_hi(n)
            act.wait_ge(banks_open, 1)
            seed(0, 0)
            seed(1, 1)
            steps(mybir.EngineType.Activation, step)

        @block.vector
        def _(dve):
            def in_ring(t):
                return x_ring[:, bass.ds((t % RING) * P, P)]

            def prepare_x(t, s):
                count = t + 1 if isinstance(t, int) else dve.snap(t + 1)
                nc.vector.tensor_copy(x_parts[:, 0, :], in_ring(t)).then_inc(x_hi_ready, 1)
                dve.wait_ge(x_hi_ready, count)
                nc.vector.tensor_tensor(x_parts[:, 1, :], in_ring(t), x_parts[:, 0, :],
                                        ALU.subtract).then_inc(x_lo_ready, 1)
                dve.wait_ge(x_lo_ready, count)
                nc.vector.transpose(xT[:, s // GROUP, :, :, :, s % GROUP],
                                    x_parts[:, :, :].rearrange("p a (k n) -> p a k n", k=J)).then_inc(xT_ready, 1)

            def stage(m, m8):
                dve.wait_ge(xw_in_psum, m + 1)
                if not isinstance(m, int) or m >= 2:
                    dve.wait_ge(xw_moved[m8 % 2], (m - m8 % 2) * (MOVE_DMA // 2))
                nc.vector.tensor_tensor(xw_stage[:, m8 % 2, :], xw_ps[m8 % 2][:, :], bias_sc[:, m8 % GROUP, :],
                                        ALU.add).then_inc(xw_staged, 1)

            def transpose_h(ready, part, to, done, count):
                dve.wait_ge(ready, count)
                nc.vector.transpose(to[:, :], part[:, :]).then_inc(done, 1)

            def step(t, s, left):
                now = t + 1 if isinstance(t, int) else dve.snap(t + 1)
                dve.wait_ge(if_ready, now)
                nc.vector.tensor_tensor(f_c[:, :], i_f[:, P:2 * P], c_state[:, :], ALU.mult)
                dve.wait_ge(g_ready, now)
                nc.vector.tensor_tensor(i_g[:, :], i_f[:, 0:P], g_gate[:, :], ALU.mult).then_inc(i_g_ready, 1)
                dve.wait_ge(i_g_ready, now)
                nc.vector.tensor_tensor(c_state[:, :], i_g[:, :], f_c[:, :], ALU.add).then_inc(c_ready, 1)
                dve.wait_ge(tanh_c_ready, now)
                if left:
                    nc.vector.tensor_tensor(h_hi[:, :], o_gate[:, :], tanh_c[:, :],
                                            ALU.mult).then_inc(h_hi_ready, 1)
                    transpose_h(h_hi_ready, h_hi, hT_hi, hT_hi_ready, t + 2)
                nc.vector.tensor_tensor(h_full[:, :], o_gate[:, :], tanh_c[:, :],
                                        ALU.mult).then_inc(h_full_ready, 1)
                dve.wait_ge(h_full_ready, now)
                if left:
                    nc.vector.tensor_tensor(h_lo[:, :], h_full[:, :], h_hi[:, :],
                                            ALU.subtract).then_inc(h_lo_ready, 1)
                    transpose_h(h_lo_ready, h_lo, hT_lo, hT_lo_ready, t + 2)
                if left >= ITEM_AHEAD:
                    stage(t + ITEM_AHEAD, (s + ITEM_AHEAD) % BODY)
                if left >= XT_AHEAD:
                    if (s + XT_AHEAD) % BODY == 0:
                        dve.wait_ge(x_loaded, (t + (XT_AHEAD + BODY)) * (X_DMA // BODY))
                    prepare_x(t + XT_AHEAD, (s + XT_AHEAD) % BODY)
                nc.vector.tensor_tensor(in_ring(t), in_ring(t), h_full[:, :], ALU.add).then_inc(out_ready, 1)

            def split_lo(n):
                dve.wait_ge(w_hi_ready, n + 1)
                src = w_raw[:, n, :].rearrange("p (g j f) -> p j g f", g=GATES, j=J)
                hi = w_hi[:, n // J, n % J, :, :].rearrange("p j (g f) -> p j g f", g=GATES)
                lo = w_lo[:, n // J, n % J, :, :].rearrange("p j (g f) -> p j g f", g=GATES)
                for j in range(J):
                    v = nc.vector.scalar_tensor_tensor(out=lo[:, j, :, :], in0=src[:, j, :, :], scalar=WSCALE,
                                                       in1=hi[:, j, :, :], op0=ALU.mult, op1=ALU.subtract)
                v.then_inc(w_lo_ready, 1)

            nc.vector.memset(c_state[:, :], 0.0).then_inc(c_zeroed, 1)
            dve.wait_ge(h0_loaded, 16)
            nc.vector.tensor_copy(h_hi[:, :], h0_raw[:, :]).then_inc(h_hi_ready, 1)
            transpose_h(h_hi_ready, h_hi, hT_hi, hT_hi_ready, 1)
            nc.vector.tensor_tensor(h_lo[:, :], h0_raw[:, :], h_hi[:, :], ALU.subtract).then_inc(h_lo_ready, 1)
            transpose_h(h_lo_ready, h_lo, hT_lo, hT_lo_ready, 1)
            dve.wait_ge(x_loaded, X_DMA)
            for t in range(2 * GROUP):
                if t:
                    dve.wait_ge(xT_ready, t)
                prepare_x(t, t)
                if t >= GROUP:
                    split_lo(t - GROUP)
            dve.wait_ge(bias_ready, 1)
            for m in range(GROUP):
                stage(m, m)
                split_lo(J + m)
            dve.wait_ge(x_loaded, 2 * X_DMA)
            for t in range(BODY, XT_AHEAD):
                dve.wait_ge(xT_ready, t)
                prepare_x(t, t % BODY)
            for m in range(GROUP, ITEM_AHEAD):
                stage(m, m)
            dve.wait_ge(c_zeroed, 1)
            steps(mybir.EngineType.DVE, step)


_INS = ['x', 'cond_1024', 'L0_cond_Wx', 'L0_cond_Wh', 'L0_cond_b']


def kernel(**inputs):
    import numpy as _np
    import concourse.bacc as _bacc
    from concourse import mybir as _mybir
    from concourse.bass_utils import run_bass_kernel_spmd as _run

    nc = _bacc.Bacc("TRN2", target_bir_lowering=False, num_devices=1)
    arrays, args = {}, []
    for name in _INS:
        a = _np.ascontiguousarray(inputs[name])
        arrays[f"in_{name}_dram"] = a
        args.append(nc.dram_tensor(f"in_{name}_dram", a.shape, _mybir.dt.from_np(a.dtype), kind="ExternalInput").ap())
    o = nc.dram_tensor("out_0_dram", inputs['x'].shape, _mybir.dt.float32, kind="ExternalOutput").ap()
    lstm_residual(nc, *args, o)
    r = _run(nc, [arrays], core_ids=[0])
    return r.results[0]["out_0_dram"]
```
